# Optimizing a Trainium2 kernel written in Bass

```python
import numpy as np
import jax
import jax.numpy as jnp

def _softmax(x, axis=-1):
    return jax.nn.softmax(x, axis=axis)
def _gelu(x):
    return jax.nn.gelu(x, approximate=True)
def _silu(x):
    return jax.nn.silu(x)
def _sigmoid(x):
    return jax.nn.sigmoid(x)
def _layernorm(x, axis=-1, eps=1e-5):
    m = jnp.mean(x, axis=axis, keepdims=True)
    v = jnp.var(x, axis=axis, keepdims=True)
    return (x - m) / jnp.sqrt(v + eps)
def _scatter_add(tgt, idx, src, axis=0):
    return tgt.at[idx].add(src)
def _segment_sum(src, seg, n):
    return jax.ops.segment_sum(src, seg, n)

kernel_name = 'mk_adj_preln_d2_adj_256_b15b07'

def setup_inputs(seed: int = 0):
    np.random.seed(seed)
    _w = jnp.asarray
    def _rec_inputs():
        import jax
        import jax.numpy as jnp
        _gk = jax.random.key(seed)
        x = 7.22e-05 + 1 * jax.random.normal(jax.random.fold_in(_gk, 1), (64, 256, 256), jnp.float32)
        _a = jax.random.bernoulli(jax.random.fold_in(_gk, 2), 0.015625, (64, 256, 256))
        _a = jnp.logical_or(_a, jnp.swapaxes(_a, -1, -2))
        _a = jnp.logical_or(_a, jnp.eye(256, dtype=bool))
        _af = _a.astype(jnp.float32)
        adj = _af
        return x, adj
    x, adj = _rec_inputs()
    def _L0_gnn_setup():
        import jax, jax.numpy as jnp
        import numpy as np
        from jax import lax
        DIM = 256
        EPS = 1e-05

        def _bn(h, g, b, m, v):
            scale = g / jnp.sqrt(v + EPS)
            return h * scale[None, :, None] + (b - m * scale)[None, :, None]

        def _conv1d(h, w, pad):
            return lax.conv_general_dilated(h, w, window_strides=(1,), padding=[(pad, pad)], dimension_numbers=('NCH', 'OIH', 'NCH'))
        key = jax.random.key(seed)
        ks = jax.random.split(key, 16)
        bs, n, d = (16, 2048, DIM)
        s = 0.05
        return {'x': jax.random.normal(ks[0], (bs, n, d), jnp.float32), 'mask': jnp.ones((bs, n, n), jnp.float32), 'w_se': jax.random.normal(ks[1], (3, d), jnp.float32) * s, 'b_se': jnp.zeros((3,), jnp.float32), 'conv1_w': jax.random.normal(ks[2], (d, d, 1), jnp.float32) * s, 'bn1_g': jnp.ones((d,), jnp.float32), 'bn1_b': jnp.zeros((d,), jnp.float32), 'bn1_m': jnp.zeros((d,), jnp.float32), 'bn1_v': jnp.ones((d,), jnp.float32), 'conv2_w': jax.random.normal(ks[3], (d, d, 17), jnp.float32) * s, 'bn2_g': jnp.ones((d,), jnp.float32), 'bn2_b': jnp.zeros((d,), jnp.float32), 'bn2_m': jnp.zeros((d,), jnp.float32), 'bn2_v': jnp.ones((d,), jnp.float32), 'w_msg': jax.random.normal(ks[4], (d, d), jnp.float32) * s, 'b_msg': jnp.zeros((d,), jnp.float32), 'w_ih': jax.random.normal(ks[5], (3 * d, 2 * d), jnp.float32) * s, 'b_ih': jnp.zeros((3 * d,), jnp.float32), 'w_hh': jax.random.normal(ks[6], (3 * d, d), jnp.float32) * s, 'b_hh': jnp.zeros((3 * d,), jnp.float32)}
    _L0_gnn_all = _L0_gnn_setup()
    _L0_gnn_in = {k: v for k, v in _L0_gnn_all.items() if k in ('w_se', 'b_se', 'conv1_w', 'bn1_g', 'bn1_b', 'bn1_m', 'bn1_v', 'conv2_w', 'bn2_g', 'bn2_b', 'bn2_m', 'bn2_v', 'w_msg', 'b_msg', 'w_ih', 'b_ih', 'w_hh', 'b_hh', )}
    del _L0_gnn_all

    def _L1_gnn_setup():
        import jax, jax.numpy as jnp
        import numpy as np
        key = jax.random.key(seed)
        k1, k2, k3 = jax.random.split(key, 3)
        b, n, d, f = (16, 2048, 256, 256)
        features = jax.random.normal(k1, (b, n, d), dtype=jnp.float32)
        A = jax.random.uniform(k2, (b, n, n), dtype=jnp.float32)
        A = A / jnp.sum(A, axis=-1, keepdims=True)
        weight = jax.random.normal(k3, (2 * d, f), dtype=jnp.float32) * (1.0 / np.sqrt(2 * d))
        bias = jnp.zeros((f,), dtype=jnp.float32)
        return {'features': features, 'A': A, 'weight': weight, 'bias': bias}
    _L1_gnn_all = _L1_gnn_setup()
    _L1_gnn_in = {k: v for k, v in _L1_gnn_all.items() if k in ('weight', 'bias', )}
    del _L1_gnn_all

    return {
        "x": x,
        "adj": adj,
        "L0_gnn_w_se": _L0_gnn_in["w_se"],
        "L0_gnn_b_se": _L0_gnn_in["b_se"],
        "L0_gnn_conv1_w": _L0_gnn_in["conv1_w"],
        "L0_gnn_bn1_g": _L0_gnn_in["bn1_g"],
        "L0_gnn_bn1_b": _L0_gnn_in["bn1_b"],
        "L0_gnn_bn1_m": _L0_gnn_in["bn1_m"],
        "L0_gnn_bn1_v": _L0_gnn_in["bn1_v"],
        "L0_gnn_conv2_w": _L0_gnn_in["conv2_w"],
        "L0_gnn_bn2_g": _L0_gnn_in["bn2_g"],
        "L0_gnn_bn2_b": _L0_gnn_in["bn2_b"],
        "L0_gnn_bn2_m": _L0_gnn_in["bn2_m"],
        "L0_gnn_bn2_v": _L0_gnn_in["bn2_v"],
        "L0_gnn_w_msg": _L0_gnn_in["w_msg"],
        "L0_gnn_b_msg": _L0_gnn_in["b_msg"],
        "L0_gnn_w_ih": _L0_gnn_in["w_ih"],
        "L0_gnn_b_ih": _L0_gnn_in["b_ih"],
        "L0_gnn_w_hh": _L0_gnn_in["w_hh"],
        "L0_gnn_b_hh": _L0_gnn_in["b_hh"],
        "L1_gnn_weight": _L1_gnn_in["weight"],
        "L1_gnn_bias": _L1_gnn_in["bias"],
    }

def reference(x, adj, L0_gnn_w_se, L0_gnn_b_se, L0_gnn_conv1_w, L0_gnn_bn1_g, L0_gnn_bn1_b, L0_gnn_bn1_m, L0_gnn_bn1_v, L0_gnn_conv2_w, L0_gnn_bn2_g, L0_gnn_bn2_b, L0_gnn_bn2_m, L0_gnn_bn2_v, L0_gnn_w_msg, L0_gnn_b_msg, L0_gnn_w_ih, L0_gnn_b_ih, L0_gnn_w_hh, L0_gnn_b_hh, L1_gnn_weight, L1_gnn_bias):
    import jax
    import jax.numpy as jnp
    def _L0_gnn_ref(x, mask, w_se, b_se, conv1_w, bn1_g, bn1_b, bn1_m, bn1_v, conv2_w, bn2_g, bn2_b, bn2_m, bn2_v, w_msg, b_msg, w_ih, b_ih, w_hh, b_hh):
        import jax, jax.numpy as jnp
        import numpy as np
        from jax import lax
        DIM = 256
        EPS = 1e-05

        def _bn(h, g, b, m, v):
            scale = g / jnp.sqrt(v + EPS)
            return h * scale[None, :, None] + (b - m * scale)[None, :, None]

        def _conv1d(h, w, pad):
            return lax.conv_general_dilated(h, w, window_strides=(1,), padding=[(pad, pad)], dimension_numbers=('NCH', 'OIH', 'NCH'))
        d = x.shape[-1]
        xc = jnp.transpose(x, (0, 2, 1))
        h = _bn(_conv1d(xc, conv1_w, 0), bn1_g, bn1_b, bn1_m, bn1_v)
        h = jax.nn.relu(h)
        h = _bn(_conv1d(h, conv2_w, 8), bn2_g, bn2_b, bn2_m, bn2_v)
        x_conv = jnp.transpose(jax.nn.relu(h + xc), (0, 2, 1))
        s = x @ w_se.T + b_se
        sq = jnp.sum(s * s, axis=-1)
        dist = sq[:, :, None] + sq[:, None, :] - 2.0 * jnp.einsum('bnd,bmd->bnm', s, s)
        A = jnp.exp(-dist) * mask
        msg = jax.nn.relu(x @ w_msg.T + b_msg)
        x_nmp = jnp.einsum('bnm,bmd->bnd', A, msg)
        x_in = jnp.concatenate([x_conv, x_nmp], axis=-1)
        gi = x_in @ w_ih.T + b_ih
        gh = x @ w_hh.T + b_hh
        gi_r, gi_z, gi_n = (gi[..., :d], gi[..., d:2 * d], gi[..., 2 * d:])
        gh_r, gh_z, gh_n = (gh[..., :d], gh[..., d:2 * d], gh[..., 2 * d:])
        r = jax.nn.sigmoid(gi_r + gh_r)
        z = jax.nn.sigmoid(gi_z + gh_z)
        nn_ = jnp.tanh(gi_n + r * gh_n)
        return (1.0 - z) * nn_ + z * x

    def _L1_gnn_ref(features, A, weight, bias):
        import jax, jax.numpy as jnp
        import numpy as np
        agg = jnp.einsum('bnm,bmd->bnd', A, features)
        d = features.shape[-1]
        out = jnp.einsum('bnd,df->bnf', features, weight[:d]) + jnp.einsum('bnd,df->bnf', agg, weight[d:]) + bias
        return jax.nn.relu(out)

    h = jnp.maximum(_layernorm(x, axis=-1), 0.0)
    x = x + _L0_gnn_ref(h, adj, L0_gnn_w_se, L0_gnn_b_se, L0_gnn_conv1_w, L0_gnn_bn1_g, L0_gnn_bn1_b, L0_gnn_bn1_m, L0_gnn_bn1_v, L0_gnn_conv2_w, L0_gnn_bn2_g, L0_gnn_bn2_b, L0_gnn_bn2_m, L0_gnn_bn2_v, L0_gnn_w_msg, L0_gnn_b_msg, L0_gnn_w_ih, L0_gnn_b_ih, L0_gnn_w_hh, L0_gnn_b_hh)
    h = jnp.maximum(_layernorm(x, axis=-1), 0.0)
    x = x + _L1_gnn_ref(h, adj, L1_gnn_weight, L1_gnn_bias)
    return x


_drawn_inputs = setup_inputs


def setup_inputs(seed=0):
    import zlib

    import numpy as np

    out = dict(_drawn_inputs(seed))
    spreads = {'L0_gnn_b_se': (0.0, 0.8),
     'L0_gnn_bn1_g': (1.0, 0.2),
     'L0_gnn_bn1_b': (0.0, 0.1),
     'L0_gnn_bn1_m': (0.0, 0.1),
     'L0_gnn_bn1_v': (1.0, 0.6),
     'L0_gnn_bn2_g': (1.0, 0.2),
     'L0_gnn_bn2_b': (0.0, 0.519),
     'L0_gnn_bn2_m': (0.0, 0.415),
     'L0_gnn_bn2_v': (1.0, 0.6),
     'L0_gnn_b_msg': (0.0, 0.1),
     'L0_gnn_b_ih': (0.0, 0.29),
     'L0_gnn_b_hh': (0.0, 0.393),
     'L1_gnn_bias': (0.0, 0.284)}
    factors = {}
    for name, (base, spread) in spreads.items():
        noise = np.random.default_rng([zlib.crc32(name.encode()), seed]).standard_normal(out[name].shape)
        drawn = base * np.exp(spread * noise) if base else spread * noise
        out[name] = jnp.asarray(drawn.astype(out[name].dtype))
    for name, factor in factors.items():
        out[name] = (out[name] * factor).astype(out[name].dtype)
    return out
```

```python
from contextlib import ExitStack

import concourse.bass as bass
from concourse import mybir

ALU = mybir.AluOpType
ACT = mybir.ActivationFunctionType
F32 = mybir.dt.float32
F32R = mybir.dt.float32r
F16 = mybir.dt.float16
U32 = mybir.dt.uint32
RMAX = bass.bass_isa.ReduceOp.max

P = 128
D = 256
N = 256
H = D // P
EPS = 1e-5
TAPS = 17
PAD = 8
G = 4
SEQ = (N + 2 * PAD) // 4
CONV_EXP = 10.0
W_EXP = 11.0
EXPONENT = 0x7F800000
ORDER = (1, 0, 2)
CHAINS = [(half, a, b) for half in range(H) for a in ORDER for b in ORDER]
PASSES = ((0, 0), (0, 1), (1, 0))


def at(j, per, n):
    return j * per + n


def subtaps(a, b):
    return 5 if a < 2 and b < 2 else 4


def convolution_weights(nc, ident, w2, w1t, cvec, conv1_w, conv2_w, bn1, bn2):
    wnat_d = conv2_w.rearrange("(h p) i k -> h p (i k)", p=P)
    w1_d = conv1_w.rearrange("(h p) i k -> p h (i k)", p=P)
    with ExitStack() as ctx:
        def sb(name, shape, dt=F32):
            return ctx.enter_context(nc.sbuf_tensor(name, shape, dt))

        def sem(name):
            return ctx.enter_context(nc.semaphore(name))

        wnat = [sb(f"wnat{h}", [P, D * TAPS]) for h in range(H)]
        taps = sb("taps", [P, H, TAPS, D])
        square = sb("square", [P, 2, D])
        summed = sb("summed", [P, 3, H, 4, D])
        w1n = sb("w1n", [P, H, D])
        par = sb("par", [P, 8, H])
        tmp = sb("tmp", [P, 12, H])
        half_power = sb("half_power", [P, 2])
        psw = [ctx.enter_context(nc.psum_tensor(f"psw{i}", [P, 512], F32)) for i in range(4)]

        loaded_w2 = [sem(f"loaded_w2_{h}") for h in range(H)]
        loaded_small = sem("loaded_small")
        ident_made = sem("ident_made")
        pool_step = sem("pool_step")
        norms_done = sem("norms_done")
        w2_norm = sem("w2_norm")
        vec_step = sem("vec_step")
        rows_scaled = sem("rows_scaled")
        turned = sem("turned")
        copied_act = sem("copied_act")
        copied_dve = sem("copied_dve")
        w1_high = sem("w1_high")
        w1_low = sem("w1_low")
        sums = sem("sums")
        high_done = sem("high_done")
        low_done = sem("low_done")
        exps = sem("exps")

        V = lambda ap, n: ap[:, n, :]
        made = [(0, 0), (0, 2), (2, 0), (2, 2), (0, 1), (2, 1), (1, 1), (1, 0), (1, 2)]
        SUMMED = [m for m in made if 1 in m]

        def phase(k):
            return taps[:, :, 0:16, :].rearrange("p h (q f) o -> p h q f o", f=4)[:, :, :, k, :]

        def filt(hl, m):
            a, b = m
            n = 4 * (3 * a + b)
            return w2[:, hl, n:n + 4, :, :].rearrange("p q h o -> p h q o")

        def source(m):
            if m in SUMMED:
                return summed[:, SUMMED.index(m) % 3, :, :, :]
            return phase(m[0] // 2 + m[1])

        TURNS = [(kh, k) for kh in range(H) for k in range(0, TAPS, 2)]

        with nc.Block() as block:
            @block.sync
            def _(sp):
                sp.dma_start(w1n[:, :, :], w1_d).then_inc(loaded_small, 16)
                for i, v in enumerate([*bn1, *bn2]):
                    sp.dma_start(par[:, i, :], v.rearrange("(h p) -> p h", p=P),
                                 allow_slow_non_contiguous=True).then_inc(loaded_small, 16)
                for h in range(H):
                    sp.dma_start(wnat[h][:, :], wnat_d[h]).then_inc(loaded_w2[h], 16)

            @block.gpsimd
            def _(pool):
                step = [0]

                def then(ins):
                    step[0] += 1
                    ins.then_inc(pool_step, 1)
                    pool.wait_ge(pool_step, step[0])

                then(pool.memset(ident[:, :], 0.0))
                pool.affine_select(out=ident[:, :], in_=ident[:, :], compare_op=ALU.not_equal, fill=1.0,
                                   base=0, pattern=[[-1, P]], channel_multiplier=1).then_inc(ident_made, 1)
                pool.memset(half_power[:, 0:2], 0.5)
                then(pool.memset(tmp[:, 11, :], -0.5))
                pool.wait_ge(loaded_small, 9 * 16)
                for n in range(2):
                    g, b, m, v = (par[:, 4 * n + i, :] for i in range(4))
                    s, o = V(tmp, 2 * n), V(tmp, 2 * n + 1)
                    then(pool.tensor_scalar(s, v, EPS, None, ALU.add))
                    then(pool.tensor_tensor(s, s, V(tmp, 11), ALU.pow))
                    then(pool.tensor_tensor(s, s, g, ALU.mult))
                    then(pool.tensor_tensor(o, m, s, ALU.mult))
                    then(pool.tensor_tensor(o, b, o, ALU.subtract))
                pool.wait_ge(norms_done, 2)
                then(pool.tensor_tensor(V(tmp, 4), V(tmp, 0), V(tmp, 0), ALU.mult))
                then(pool.tensor_tensor(V(tmp, 4), V(tmp, 4), V(tmp, 5), ALU.mult))
                then(pool.tensor_scalar(V(tmp, 4), V(tmp, 4), 2.0 * D, None, ALU.mult))
                then(pool.tensor_tensor(V(tmp, 6), V(tmp, 1), V(tmp, 1), ALU.mult))
                then(pool.tensor_scalar(V(tmp, 6), V(tmp, 6), 2.0, None, ALU.mult))
                then(pool.tensor_tensor(V(tmp, 4), V(tmp, 4), V(tmp, 6), ALU.add))
                then(pool.tensor_tensor(tmp[:, 6, 0:1], tmp[:, 4, 0:1], tmp[:, 4, 1:2], ALU.add))
                then(pool.tensor_tensor(tmp[:, 6, 0:1], tmp[:, 6, 0:1], half_power[:, 0:1], ALU.pow))
                then(pool.partition_all_reduce(tmp[:, 6, 1:2], tmp[:, 6, 0:1], P, RMAX))
                pool.tensor_scalar(tmp[:, 7, 0:1], tmp[:, 6, 1:2], 1e-30, None, ALU.add).then_inc(exps, 1)
                pool.wait_ge(w2_norm, 2)
                then(pool.tensor_tensor(V(tmp, 8), V(tmp, 8), half_power[:, :], ALU.pow))
                pool.tensor_scalar(V(tmp, 8), V(tmp, 8), 1e-30, None, ALU.add).then_inc(exps, 1)
                pool.wait_ge(ident_made, 1)
                for n, m in enumerate(made[:4]):
                    pool.wait_ge(high_done, n + 1)
                    pool.tensor_tensor(filt(1, m), source(m), filt(0, m), ALU.subtract)

            @block.scalar
            def _(act):
                for h in range(H):
                    act.wait_ge(loaded_w2[h], 16)
                    act.activation(taps[:, :, :, :].rearrange("p h k o -> p h (k o)")[:, h, :],
                                   wnat[h][:, :], ACT.Square, accum_out=tmp[:, 8, h:h + 1]).then_inc(w2_norm, 1)
                act.wait_ge(turned, 1)
                act.activation(w1t[:, 0, :, :].rearrange("p h o -> p (h o)"), psw[3][:, :],
                               ACT.Copy).then_inc(w1_high, 1)
                for n, (kh, k) in enumerate(TURNS):
                    if n % 2 == 0:
                        act.wait_ge(turned, n + 2)
                        w = min(2, TAPS - k)
                        act.activation(taps[:, kh, k:k + w, :],
                                       psw[n % 3][:, 0:w * D].rearrange("p (k o) -> p k o", o=D),
                                       ACT.Copy).then_inc(copied_act, 1)
                act.wait_ge(copied_act, len(TURNS) - len(TURNS) // 2)
                act.wait_ge(copied_dve, len(TURNS) // 2)
                for n, m in enumerate(made):
                    if m in SUMMED:
                        act.wait_ge(sums, SUMMED.index(m) + 1)
                    act.activation(filt(0, m), source(m), ACT.Copy).then_inc(high_done, 1)
                act.activation(w2[:, 0, 36, :, :], taps[:, :, 16, :], ACT.Copy).then_inc(high_done, 1)

            @block.vector
            def _(dve):
                step = [0]

                def then(ins):
                    step[0] += 1
                    ins.then_inc(vec_step, 1)
                    dve.wait_ge(vec_step, step[0])

                dve.wait_ge(loaded_small, 9 * 16)
                for h in range(H):
                    dve.tensor_tensor_reduce(out=square[:, h, :], in0=w1n[:, h, :], in1=w1n[:, h, :], scale=1.0,
                                             scalar=0.0, op0=ALU.mult, op1=ALU.add,
                                             accum_out=tmp[:, 5, h:h + 1]).then_inc(norms_done, 1)
                dve.wait_ge(exps, 1)
                then(dve.tensor_scalar(tmp[:, 7, 1:2].bitcast(U32), tmp[:, 7, 0:1].bitcast(U32), EXPONENT, None,
                                       ALU.bitwise_and))
                then(dve.reciprocal(tmp[:, 7, 0:1], tmp[:, 7, 1:2]))
                then(dve.tensor_scalar(tmp[:, 7, 0:1], tmp[:, 7, 0:1], 2.0 ** CONV_EXP, None, ALU.mult))
                dve.tensor_scalar(cvec[:, 0:2], V(tmp, 0), tmp[:, 7, 0:1], None, ALU.mult)
                dve.tensor_scalar(cvec[:, 2:4], V(tmp, 1), tmp[:, 7, 0:1], None, ALU.mult)
                dve.wait_ge(exps, 2)
                then(dve.tensor_scalar(V(tmp, 9).bitcast(U32), V(tmp, 8).bitcast(U32), EXPONENT, None,
                                       ALU.bitwise_and))
                then(dve.reciprocal(V(tmp, 10), V(tmp, 9)))
                then(dve.tensor_scalar(V(tmp, 10), V(tmp, 10), 2.0 ** W_EXP, None, ALU.mult))
                for h in range(H):
                    dve.tensor_scalar(wnat[h][:, :], wnat[h][:, :], tmp[:, 10, h:h + 1], None,
                                      ALU.mult).then_inc(rows_scaled, 1)
                then(dve.tensor_scalar(V(tmp, 9), V(tmp, 9), 2.0 ** -(W_EXP + CONV_EXP), tmp[:, 7, 1:2],
                                       ALU.mult, ALU.mult))
                dve.tensor_tensor(cvec[:, 4:6], V(tmp, 2), V(tmp, 9), ALU.mult)
                dve.tensor_copy(cvec[:, 6:8], V(tmp, 3))
                dve.wait_ge(w1_high, 1)
                dve.tensor_tensor(w1t[:, 1, :, :].rearrange("p h o -> p (h o)"), psw[3][:, :],
                                  w1t[:, 0, :, :].rearrange("p h o -> p (h o)").bitcast(F32),
                                  ALU.subtract).then_inc(w1_low, 1)
                for n, (kh, k) in enumerate(TURNS):
                    if n % 2 == 1:
                        dve.wait_ge(turned, n + 2)
                        w = min(2, TAPS - k)
                        dve.tensor_copy(taps[:, kh, k:k + w, :],
                                        psw[n % 3][:, 0:w * D].rearrange("p (k o) -> p k o", o=D)).then_inc(copied_dve, 1)
                dve.wait_ge(copied_act, len(TURNS) - len(TURNS) // 2)
                dve.wait_ge(copied_dve, len(TURNS) // 2)
                terms = {(0, 1): (phase(0), phase(2)), (2, 1): (phase(1), phase(3)),
                         (1, 1): (source((0, 1)), source((2, 1))),
                         (1, 0): (phase(0), phase(1)), (1, 2): (phase(2), phase(3))}
                for n, m in enumerate(SUMMED):
                    dve.tensor_tensor(source(m), *terms[m], ALU.add).then_inc(sums, 1)
                    dve.wait_ge(sums, n + 1)
                    dve.wait_ge(high_done, 5 + n)
                    dve.tensor_tensor(filt(1, m), source(m), filt(0, m), ALU.subtract).then_inc(low_done, 1)
                dve.wait_ge(high_done, len(made) + 1)
                dve.tensor_tensor(w2[:, 1, 36, :, :], taps[:, :, 16, :], w2[:, 0, 36, :, :], ALU.subtract)

            @block.tensor
            def _(pe):
                pe.wait_ge(ident_made, 1)
                pe.wait_ge(loaded_small, 9 * 16)
                for kh in range(H):
                    for oh in range(H):
                        last = pe.transpose(psw[3][:, kh * D + oh * P:kh * D + oh * P + P],
                                            w1n[:, oh, kh * P:kh * P + P], ident[:, :])
                last.then_inc(turned, 1)
                pe.wait_ge(rows_scaled, 2)
                rows = [w[:, :].rearrange("p (i k) -> p k i", k=TAPS) for w in wnat]
                for n, (kh, k) in enumerate(TURNS):
                    if n >= 3 and n % 2 == 0:
                        pe.wait_ge(copied_dve, (n - 3) // 2 + 1)
                    if n >= 3 and n % 2 == 1:
                        pe.wait_ge(copied_act, (n - 3) // 2 + 1)
                    for w in range(min(2, TAPS - k)):
                        for oh in range(H):
                            last = pe.transpose(psw[n % 3][:, w * D + oh * P:w * D + oh * P + P],
                                                rows[oh][:, k + w, kh * P:kh * P + P], ident[:, :])
                    last.then_inc(turned, 1)


def convolution(nc, ident, w2, w1t, cvec, x, conv_out):
    groups = x.shape[0] // G
    pairs = groups // 2
    x_d = x.rearrange("g (t p) d -> g p t d", p=P)
    with ExitStack() as ctx:
        def sb(name, shape, dt=F32):
            return ctx.enter_context(nc.sbuf_tensor(name, shape, dt))

        def ps(name):
            return ctx.enter_context(nc.psum_tensor(name, [P, 512], F32))

        def sem(name):
            return ctx.enter_context(nc.semaphore(name))

        xin = sb("xin", [P, 2, H, D])
        xhat = sb("xhat", [P, 2, H, D])
        stats = sb("stats", [P, 2, H, 6])
        meanvar = sb("meanvar", [P, 2, H, 2])
        rstd = sb("rstd", [P, 2, H])
        minus_half = sb("minus_half", [P, H])
        eps = sb("eps", [P, H])
        wait_taker = sb("wait_taker", [P, 1])
        ht = sb("ht", [P, 2, 2, G, H, N], F32R)
        c1 = sb("c1", [P, 2, 4, H, SEQ])
        outer = sb("outer", [P, 3, 2, H, SEQ])
        inner = sb("inner", [P, 2, 3, H, SEQ])
        seqs = sb("seqs", [P, 2, 2, 3, 3, H, G, SEQ], F16)
        middle = sb("middle", [P, 256])
        za = sb("za", [P, H, 2, 2, 256])
        v = sb("v", [P, G * N])
        xc = sb("xc", [P, 2, G * N])

        chain_ps = [ps(f"chain_ps{b}") for b in range(3)]
        turn_ps = ps("turn_ps")
        c1_ps = ps("c1_ps")

        x_loaded = [sem(f"x_loaded{i}") for i in range(2)]
        stats_done = sem("stats_done")
        rstd_done = sem("rstd_done")
        xhat_done = sem("xhat_done")
        turned = sem("turned")
        h_high = sem("h_high")
        h_low = sem("h_low")
        conv1_done = sem("conv1_done")
        c1_done = sem("c1_done")
        outer_pool = sem("outer_pool")
        outer_act = sem("outer_act")
        outer_dve = sem("outer_dve")
        inner_done = sem("inner_done")
        high_done = sem("high_done")
        low_pool = sem("low_pool")
        low_dve = sem("low_dve")
        cleared = sem("cleared")
        chain_done = sem("chain_done")
        middle_done = sem("middle_done")
        side_done = [sem(f"side_done{b}") for b in (0, 2)]
        y_done = [sem(f"y_done{h}") for h in range(H)]
        v_done = sem("v_done")
        xc_done = sem("xc_done")
        xc_stored = [sem(f"xc_stored{i}") for i in range(2)]
        local_pool = sem("local_pool")
        local_dve = sem("local_dve")

        def f_count(j, u, b, n=1, per=1):
            return at(j, 2 * G * per, (G * (u + 1) + b) * per + n)

        def load_x(sp, j, u, b):
            f = at(j, 2 * G, G * (u + 1) + b)
            if not (isinstance(j, int) and f < 2):
                sp.wait_ge(xhat_done, f_count(j, u, b, -1))
            sp.dma_start(xin[:, b % 2, :, :], x_d[f]).then_inc(x_loaded[b % 2], 16)

        def layer_stats(dve, j, u, b):
            dve.wait_ge(x_loaded[b % 2], at(j, 16 * G, 16 * (G * (u + 1) // 2 + b // 2 + 1)))
            for t in range(H):
                dve.bn_stats(stats[:, b % 2, t, :], xin[:, b % 2, t, :]).then_inc(local_dve, 1)
            dve.wait_ge(local_dve, f_count(j, u, b, 2, 2))
            dve.memset(wait_taker[:, :], 0.0)
            for t in range(H):
                last = dve.bn_aggr(meanvar[:, b % 2, t, :], stats[:, b % 2, t, :])
            last.then_inc(stats_done, 1)

        def layer_rstd(pool, j, u, b):
            pool.wait_ge(stats_done, f_count(j, u, b))
            pool.tensor_tensor(rstd[:, b % 2, :], meanvar[:, b % 2, :, 1], eps[:, :], ALU.add).then_inc(local_pool, 1)
            pool.wait_ge(local_pool, f_count(j, u, b, 1))
            pool.tensor_tensor(rstd[:, b % 2, :], rstd[:, b % 2, :], minus_half[:, :], ALU.pow).then_inc(rstd_done, 1)

        def normalise(dve, j, u, b):
            dve.wait_ge(rstd_done, f_count(j, u, b))
            if not (isinstance(j, int) and at(j, 2 * G, G * (u + 1) + b) < 2):
                dve.wait_ge(turned, f_count(j, u, b, -1))
            for t in range(H):
                last = dve.tensor_scalar(xhat[:, b % 2, t, :], xin[:, b % 2, t, :], meanvar[:, b % 2, t, 0:1],
                                         rstd[:, b % 2, t:t + 1], ALU.subtract, ALU.mult)
            last.then_inc(xhat_done, 1)

        def turn_h(pe, j, u, b):
            pe.wait_ge(xhat_done, f_count(j, u, b))
            if not (isinstance(j, int) and at(j, 2 * G, G * (u + 1) + b) < 1):
                pe.wait_ge(h_low, f_count(j, u, b, 0))
            for kh in range(H):
                for t in range(H):
                    last = pe.transpose(turn_ps[:, kh * N + t * P:kh * N + t * P + P],
                                        xhat[:, b % 2, t, kh * P:kh * P + P], ident[:, :])
            last.then_inc(turned, 1)

        def split_h_high(act, j, u, b):
            act.wait_ge(turned, f_count(j, u, b))
            if u >= 0:
                act.wait_ge(v_done, c_count(j, u, 0, 4))
            act.activation(ht[:, (u + 1) % 2, 0, b, :, :].rearrange("p h n -> p (h n)"), turn_ps[:, :],
                           ACT.Relu).then_inc(h_high, 1)

        def split_h_low(dve, j, u, b):
            dve.wait_ge(h_high, f_count(j, u, b))
            dve.scalar_tensor_tensor(out=ht[:, (u + 1) % 2, 1, b, :, :].rearrange("p h n -> p (h n)"), in0=turn_ps[:, :],
                                     scalar=0.0, in1=ht[:, (u + 1) % 2, 0, b, :, :].rearrange("p h n -> p (h n)").bitcast(F32),
                                     op0=ALU.max, op1=ALU.subtract).then_inc(h_low, 1)

        def conv1(pe, j, u, b):
            pe.wait_ge(h_low, f_count(j, u, b))
            if not (isinstance(j, int) and at(j, 2 * G, G * (u + 1) + b) < 1):
                pe.wait_ge(c1_done, f_count(j, u, b, 0))
            for oh in range(H):
                for kh in range(H):
                    for n, (wl, dl) in enumerate(PASSES):
                        last = pe.matmul(c1_ps[:, oh * N:oh * N + N], w1t[:, wl, kh, oh * P:oh * P + P],
                                         ht[:, (u + 1) % 2, dl, b, kh, :], start=(kh == 0 and n == 0),
                                         stop=(kh == H - 1 and n == 2))
            last.then_inc(conv1_done, 1)

        def conv1_out(act, j, u, b):
            act.wait_ge(conv1_done, f_count(j, u, b))
            if not (isinstance(j, int) and at(j, 2 * G, G * (u + 1) + b) < 2):
                act.wait_ge(outer_pool, f_count(j, u, b, -1))
                act.wait_ge(outer_dve, f_count(j, u, b, -1))
            for oh in range(H):
                last = act.activation(c1[:, b % 2, :, oh, PAD // 4:PAD // 4 + N // 4],
                                      c1_ps[:, oh * N:oh * N + N].rearrange("p (i f) -> p f i", f=4), ACT.Relu,
                                      scale=cvec[:, oh:oh + 1], bias=cvec[:, 2 + oh:3 + oh])
            last.then_inc(c1_done, 1)
            act.wait_ge(c1_done, f_count(j, u, b))
            if not (isinstance(j, int) and at(j, 2 * G, G * (u + 1) + b) < 1):
                act.wait_ge(inner_done, f_count(j, u, b, 0, 2))
                act.wait_ge(low_pool, f_count(j, u, b, 0, 2))
            act.activation(outer[:, 1, :, :, :], c1[:, b % 2, 1:4:2, :, :], ACT.Copy).then_inc(outer_act, 1)

        def outer_differences_pool(pool, j, u, b):
            pool.wait_ge(c1_done, f_count(j, u, b))
            if not (isinstance(j, int) and at(j, 2 * G, G * (u + 1) + b) < 1):
                pool.wait_ge(inner_done, f_count(j, u, b, 0, 2))
                pool.wait_ge(high_done, f_count(j, u, b, 0, 3))
            pool.tensor_tensor(outer[:, 0, :, :, :], c1[:, b % 2, 0:4:2, :, :], c1[:, b % 2, 1:4:2, :, :],
                               ALU.subtract).then_inc(outer_pool, 1)

        def outer_differences_dve(dve, j, u, b):
            dve.wait_ge(c1_done, f_count(j, u, b))
            if not (isinstance(j, int) and at(j, 2 * G, G * (u + 1) + b) < 1):
                dve.wait_ge(high_done, f_count(j, u, b, 0, 3))
                dve.wait_ge(low_pool, f_count(j, u, b, 0, 2))
            dve.tensor_tensor(outer[:, 2, 0, :, :], c1[:, b % 2, 2, :, :], c1[:, b % 2, 1, :, :], ALU.subtract)
            dve.tensor_tensor(outer[:, 2, 1, :, 0:SEQ - 1], c1[:, b % 2, 0, :, 1:SEQ], c1[:, b % 2, 3, :, 0:SEQ - 1],
                              ALU.subtract).then_inc(outer_dve, 1)

        def inner_differences(dve, j, u, b):
            dve.wait_ge(outer_pool, f_count(j, u, b))
            dve.wait_ge(outer_act, f_count(j, u, b))
            dve.wait_ge(outer_dve, f_count(j, u, b))
            dve.tensor_tensor(inner[:, 0, :, :, :], outer[:, :, 0, :, :], outer[:, :, 1, :, :],
                              ALU.subtract).then_inc(inner_done, 1)
            dve.tensor_tensor(inner[:, 1, :, :, 0:SEQ - 1], outer[:, :, 0, :, 1:SEQ], outer[:, :, 1, :, 0:SEQ - 1],
                              ALU.subtract).then_inc(inner_done, 1)

        def sequence(u, hl, pb, b, w):
            return seqs[:, (u + 1) % 2, hl, :, pb, :, b, 0:w]

        SPLITS = ((1, SEQ), (0, SEQ), (2, SEQ - 1))

        def unsplit(pb, w):
            return outer[:, :, 1, :, 0:w] if pb == 1 else inner[:, pb // 2, :, :, 0:w]

        def split_high(act, j, u, b):
            for n, (pb, w) in enumerate(SPLITS):
                if n == 0:
                    act.wait_ge(outer_pool, f_count(j, u, b))
                    act.wait_ge(outer_dve, f_count(j, u, b))
                    act.wait_ge(outer_act, f_count(j, u, b))
                else:
                    act.wait_ge(inner_done, f_count(j, u, b, n, 2))
                act.activation(sequence(u, 0, pb, b, w), unsplit(pb, w), ACT.Copy).then_inc(high_done, 1)

        def split_low_pool(pool, j, u, b):
            for n, (pb, w) in enumerate(SPLITS[:2]):
                pool.wait_ge(high_done, f_count(j, u, b, n + 1, 3))
                pool.tensor_tensor(sequence(u, 1, pb, b, w), unsplit(pb, w), sequence(u, 0, pb, b, w),
                                   ALU.subtract).then_inc(low_pool, 1)

        def split_low_dve(dve, j, u, b):
            pb, w = SPLITS[2]
            dve.wait_ge(high_done, f_count(j, u, b, 3, 3))
            dve.tensor_tensor(sequence(u, 1, pb, b, w), unsplit(pb, w), sequence(u, 0, pb, b, w),
                              ALU.subtract).then_inc(low_dve, 1)

        def c_count(j, u, n, per=len(CHAINS)):
            return at(j, 2 * per, u * per + n)

        def chain(pe, j, u, c):
            oh, a, b = CHAINS[c]
            if c == 0:
                pe.wait_ge(low_pool, f_count(j, u - 1, G - 1, 2, 2))
                pe.wait_ge(low_dve, f_count(j, u - 1, G - 1))
            read = middle_done if b == 1 else side_done[b // 2]
            pe.wait_ge(read, c_count(j, u, c // 3, 6))
            steps = [(q, kh, wl, dl) for q in range(subtaps(a, b)) for kh in range(H) for wl, dl in PASSES]
            for n, (q, kh, wl, dl) in enumerate(steps):
                w = 36 if q == 4 else 4 * (3 * a + b) + q
                last = pe.matmul(chain_ps[b][:, 0:G * 64].rearrange("p (g i) -> p g i", g=G),
                                 w2[:, wl, w, kh, oh * P:oh * P + P], seqs[:, u, dl, a, b, kh, :, q:q + 64],
                                 start=(n == 0), stop=(n == len(steps) - 1))
            last.then_inc(chain_done, 1)

        def read_middle(act, j, u, c):
            oh, a, b = CHAINS[c]
            act.wait_ge(chain_done, c_count(j, u, c + 1))
            for side in side_done:
                act.wait_ge(side, c_count(j, u, c // 3, 6))
            bias = cvec[:, 6 + oh:7 + oh] if a == 1 else 0.0
            act.activation(middle[:, :], chain_ps[b][:, 0:256], ACT.Identity,
                           scale=cvec[:, 4 + oh:5 + oh], bias=bias).then_inc(middle_done, 1)

        def read_side(dve, j, u, c):
            oh, a, b = CHAINS[c]
            dve.wait_ge(chain_done, c_count(j, u, c + 1))
            dve.wait_ge(middle_done, c_count(j, u, c // 3 + 1, 6))
            if b == 0 and a == 2:
                dve.wait_ge(y_done[oh], c_count(j, u, 1, 2))
            if b == 0 and a == 1:
                dve.wait_ge(y_done[oh], c_count(j, u, 0, 2))
            dve.scalar_tensor_tensor(out=za[:, oh, 0 if a == 1 else 1, b // 2, :], in0=chain_ps[b][:, 0:256],
                                     scalar=cvec[:, 4 + oh:5 + oh], in1=middle[:, :],
                                     op0=ALU.mult, op1=ALU.add).then_inc(side_done[b // 2], 1)

        def outer_phase(pool, j, u, c):
            oh, a, b = CHAINS[c]
            for side in side_done:
                pool.wait_ge(side, c_count(j, u, c // 3 + 1, 6))
            if a == 0:
                pool.wait_ge(xc_done, c_count(j, u, oh, 2))
            pool.tensor_tensor(v[:, :].rearrange("p (i b a) -> p a b i", a=2, b=2)[:, a // 2, :, :],
                               za[:, oh, 1, :, :], za[:, oh, 0, :, :], ALU.add).then_inc(y_done[oh], 1)
            if a == 2:
                vv = v[:, :].rearrange("p (g n) -> p g n", g=G)
                pool.wait_ge(y_done[oh], c_count(j, u, 2, 2))
                for hl in range(2):
                    pool.tensor_tensor(vv, vv, ht[:, u, hl, :, oh, :].bitcast(F32), ALU.add).then_inc(v_done, 1)
                    pool.wait_ge(v_done, c_count(j, u, 2 * oh + hl + 1, 4))

        def relu_out(act, j, u, oh):
            act.wait_ge(v_done, c_count(j, u, 2 * oh + 2, 4))
            act.wait_ge(xc_stored[oh], c_count(j, u, 0, 16))
            act.activation(xc[:, oh, :], v[:, :], ACT.Relu).then_inc(xc_done, 1)

        def store_out(sp, j, u, oh):
            sp.wait_ge(xc_done, c_count(j, u, oh + 1, 2))
            sp.dma_start(conv_out[at(j, 2, u), :, oh].rearrange("b p n -> p b n"),
                         xc[:, oh, :].rearrange("p (b n) -> p b n", n=N)).then_inc(xc_stored[oh], 16)

        def loop(engine, body):
            body(0, pairs == 1)
            if pairs == 1:
                return
            if pairs > 2:
                with engine.Fori(1, pairs - 1) as j:
                    body(j, False)
            body(pairs - 1, True)

        with nc.Block() as block:
            @block.sync
            def _(sp):
                for b in range(G):
                    load_x(sp, 0, -1, b)

                def body(j, last):
                    for u in range(2):
                        for c in range(len(CHAINS)):
                            if c % G == 0 and c < 4 * G and not (last and u == 1):
                                load_x(sp, j, u, c // G)
                            if c == 12:
                                store_out(sp, j, u, 0)
                        store_out(sp, j, u, 1)

                loop(sp, body)
                for oh in range(H):
                    sp.wait_ge(xc_stored[oh], 16 * groups)

            @block.gpsimd
            def _(pool):
                pool.memset(minus_half[:, :], -0.5).then_inc(cleared, 1)
                pool.memset(eps[:, :], EPS).then_inc(cleared, 1)
                pool.wait_ge(cleared, 4)
                for b in range(G):
                    layer_rstd(pool, 0, -1, b)
                    outer_differences_pool(pool, 0, -1, b)
                    split_low_pool(pool, 0, -1, b)

                def body(j, last):
                    for u in range(2):
                        for c in range(len(CHAINS)):
                            oh, a, b = CHAINS[c]
                            if not (last and u == 1):
                                if c % 4 == 0 and c < 16:
                                    layer_rstd(pool, j, u, c // 4)
                                if c % 4 == 3 and c < 16:
                                    outer_differences_pool(pool, j, u, c // 4)
                                    split_low_pool(pool, j, u, c // 4)
                            if b == 2 and a != 1:
                                outer_phase(pool, j, u, c)

                loop(pool, body)

            @block.scalar
            def _(act):
                act.wait_ge(cleared, 4)
                for b in range(G):
                    split_h_high(act, 0, -1, b)
                    conv1_out(act, 0, -1, b)
                    split_high(act, 0, -1, b)

                def body(j, last):
                    for u in range(2):
                        for c in range(len(CHAINS)):
                            oh, a, b = CHAINS[c]
                            if b == 1:
                                read_middle(act, j, u, c)
                            if c == 12:
                                relu_out(act, j, u, 0)
                            if not (last and u == 1):
                                if c % 4 == 1 and c < 16:
                                    split_h_high(act, j, u, c // 4)
                                if c % 4 == 2 and c < 16:
                                    conv1_out(act, j, u, c // 4)
                                if c % 4 == 3 and c < 16:
                                    split_high(act, j, u, c // 4)
                        relu_out(act, j, u, 1)

                loop(act, body)

            @block.vector
            def _(dve):
                dve.memset(c1[:, :, :, :, :].rearrange("p s f h i -> p (s f h i)"), 0.0).then_inc(cleared, 1)
                dve.memset(outer[:, :, :, :, :].rearrange("p a s h i -> p (a s h i)"), 0.0).then_inc(cleared, 1)
                dve.wait_ge(cleared, 4)
                for b in range(G):
                    layer_stats(dve, 0, -1, b)
                    normalise(dve, 0, -1, b)
                    split_h_low(dve, 0, -1, b)
                    outer_differences_dve(dve, 0, -1, b)
                    inner_differences(dve, 0, -1, b)
                    split_low_dve(dve, 0, -1, b)

                def body(j, last):
                    for u in range(2):
                        for c in range(len(CHAINS)):
                            oh, a, b = CHAINS[c]
                            more = not (last and u == 1) and c < 16
                            if more and c == 0:
                                layer_stats(dve, j, u, 0)
                            if b != 1:
                                read_side(dve, j, u, c)
                            if more and c % 4 == 0:
                                normalise(dve, j, u, c // 4)
                            if more and c % 4 == 1:
                                split_h_low(dve, j, u, c // 4)
                            if more and c % 4 == 3:
                                outer_differences_dve(dve, j, u, c // 4)
                                inner_differences(dve, j, u, c // 4)
                                split_low_dve(dve, j, u, c // 4)
                                if c < 12:
                                    layer_stats(dve, j, u, c // 4 + 1)

                loop(dve, body)

            @block.tensor
            def _(pe):
                for b in range(G):
                    turn_h(pe, 0, -1, b)
                    conv1(pe, 0, -1, b)

                def body(j, last):
                    for u in range(2):
                        for c in range(len(CHAINS)):
                            chain(pe, j, u, c)
                            if not (last and u == 1) and c < 16:
                                if c % 4 == 1:
                                    turn_h(pe, j, u, c // 4)
                                if c % 4 == 2:
                                    conv1(pe, j, u, c // 4)

                loop(pe, body)


def gate_weights(nc, ident, w, a):
    with ExitStack() as ctx:
        def sb(name, shape, dt=F32):
            return ctx.enter_context(nc.sbuf_tensor(name, shape, dt))

        def sem(name):
            return ctx.enter_context(nc.semaphore(name))

        ih = sb("ih", [P, 6, 2 * D])
        hh = sb("hh", [P, 6, D])
        msg = sb("msg_w", [P, H, D])
        l1 = sb("l1", [P, 4, D])
        se = sb("se", [P, H, P])
        bias_hh = sb("bias_hh", [P, 3 * D])
        psw = [ctx.enter_context(nc.psum_tensor(f"pst{i}", [P, 512], F32)) for i in range(4)]
        loaded = sem("loaded")
        loaded_se = sem("loaded_se")
        zeroed = sem("zeroed")
        turned = sem("turned_w")
        high = sem("high_w")
        low = sem("low_w")

        banks = []
        for k in range(0, 4, 2):
            for o in range(0, 6, 2):
                banks.append((ih, k, o, lambda hl, k=k, o=o: w["ih"][:, hl, k:k + 2, o * P:o * P + D]))
        for o in range(0, 6, 2):
            banks.append((hh, 0, o, lambda hl, o=o: w["hh"][:, hl, :, o * P:o * P + D]))
        banks.append((msg, 0, 0, lambda hl: w["msg"][:, hl, :, :]))

        with nc.Block() as block:
            @block.sync
            def _(sp):
                sp.dma_start(ih[:, :, :], a["w_ih"].rearrange("(t p) k -> p t k", p=P)).then_inc(loaded, 16)
                sp.dma_start(hh[:, :, :], a["w_hh"].rearrange("(t p) k -> p t k", p=P)).then_inc(loaded, 16)
                sp.dma_start(msg[:, :, :], a["w_msg"].rearrange("(t p) k -> p t k", p=P)).then_inc(loaded, 16)
                sp.dma_start(l1[:, :, :], a["l1_w"].rearrange("(t p) f -> p t f", p=P)).then_inc(loaded, 16)
                sp.dma_start(w["bias_n"][:, 0:D], a["b_ih"][2 * D:3 * D].partition_broadcast(P)).then_inc(loaded, 16)
                sp.dma_start(w["bias_n"][:, D:2 * D], a["b_hh"][2 * D:3 * D].partition_broadcast(P)).then_inc(loaded, 16)
                sp.dma_start(w["bias_rz"][:, :], a["b_ih"][0:2 * D].partition_broadcast(P)).then_inc(loaded, 16)
                sp.dma_start(bias_hh[:, :], a["b_hh"].partition_broadcast(P)).then_inc(loaded, 16)
                sp.dma_start(w["bias_out"][:, :], a["l1_b"].partition_broadcast(P)).then_inc(loaded, 16)
                for t in range(H):
                    sp.dma_start(w["bias_msg"][:, t, :], a["b_msg"].partition_broadcast(P)).then_inc(loaded, 16)
                sp.wait_ge(zeroed, 2)
                for r in range(3):
                    for kh in range(H):
                        sp.dma_start(se[:, kh, 32 * r:32 * r + 3],
                                     a["w_se"][:, kh * P:kh * P + P].rearrange("c p -> p c"),
                                     allow_slow_non_contiguous=True).then_inc(loaded_se, 16)
                    sp.dma_start(w["bias_se"][32 * r:32 * r + 3, :], a["b_se"].rearrange("(c a) -> c a", a=1),
                                 allow_slow_non_contiguous=True).then_inc(loaded_se, 16)

            @block.scalar
            def _(act):
                act.wait_ge(loaded_se, 9 * 16)
                act.activation(w["se"][:, 0, :, :], se[:, :, :], ACT.Copy).then_inc(high, 1)
                act.wait_ge(loaded, 11 * 16)
                l1v = l1[:, :, :].rearrange("p (s h) f -> p h s f", s=2)
                act.activation(w["l1"][:, 0, :, :].rearrange("p h (s f) -> p h s f", s=2), l1v,
                               ACT.Copy).then_inc(high, 1)
                for n, (_, _, _, dest) in enumerate(banks):
                    act.wait_ge(turned, n + 1)
                    act.activation(dest(0), psw[n % 4][:, :].rearrange("p (h o) -> p h o", h=2),
                                   ACT.Copy).then_inc(high, 1)

            @block.vector
            def _(dve):
                dve.memset(se[:, :, :], 0.0).then_inc(zeroed, 1)
                dve.memset(w["bias_se"][:, :], 0.0).then_inc(zeroed, 1)
                dve.wait_ge(high, 1)
                dve.tensor_tensor(w["se"][:, 1, :, :], se[:, :, :], w["se"][:, 0, :, :].bitcast(F32), ALU.subtract)
                dve.wait_ge(high, 2)
                l1v = l1[:, :, :].rearrange("p (s h) f -> p h s f", s=2)
                high_l1 = w["l1"][:, 0, :, :].rearrange("p h (s f) -> p h s f", s=2)
                dve.tensor_tensor(w["l1"][:, 1, :, :].rearrange("p h (s f) -> p h s f", s=2), l1v,
                                  high_l1.bitcast(F32), ALU.subtract)
                dve.tensor_tensor(w["bias_rz"][:, :], w["bias_rz"][:, :], bias_hh[:, 0:2 * D], ALU.add)
                for n, (_, _, _, dest) in enumerate(banks):
                    dve.wait_ge(high, n + 3)
                    dve.tensor_tensor(dest(1), psw[n % 4][:, :].rearrange("p (h o) -> p h o", h=2),
                                      dest(0).bitcast(F32), ALU.subtract).then_inc(low, 1)

            @block.tensor
            def _(pe):
                pe.wait_ge(loaded, 11 * 16)
                for n, (src, k, o, _) in enumerate(banks):
                    if n >= 4:
                        pe.wait_ge(low, n - 3)
                    for kh in range(2):
                        for t in range(2):
                            last = pe.transpose(psw[n % 4][:, kh * D + t * P:kh * D + t * P + P],
                                                src[:, o + t, (k + kh) * P:(k + kh) * P + P], ident[:, :])
                    last.then_inc(turned, 1)


def gates(nc, ident, w, x, adj, conv_out, out):
    graphs = x.shape[0]
    x_d = x.rearrange("g (t p) d -> g p t d", p=P)
    adj_d = adj.rearrange("g (t p) m -> g p t m", p=P)
    out_d = out.rearrange("g (t p) d -> g p t d", p=P)
    conv_d = conv_out.rearrange("g b h p n -> (g b) h p n")
    with ExitStack() as ctx:
        def sb(name, shape, dt=F32):
            return ctx.enter_context(nc.sbuf_tensor(name, shape, dt))

        def ps(name):
            return ctx.enter_context(nc.psum_tensor(name, [P, 512], F32))

        def sem(name):
            return ctx.enter_context(nc.semaphore(name))

        xin = sb("xin2", [P, 2, H, D])
        xhat = sb("xhat2", [P, 2, H, D])
        adj_in = sb("adj_in", [P, 2, H, N])
        conv_in = sb("conv_in", [P, 2, H, N])
        ht = sb("ht2", [P, 2, 2, H, N], F32R)
        conv_t = sb("conv_t", [P, 2, 2, H, N], F32R)
        adj_t = sb("adj_t", [P, 2, 2, H, N], F32R)
        x1 = sb("x1", [P, 2, H, D])
        stats = sb("stats2", [P, 2, H, 6])
        meanvar = sb("meanvar2", [P, 2, H, 2])
        rstd = sb("rstd2", [P, 2, H])
        stats_b = sb("stats_b", [P, H, 6])
        meanvar_b = sb("meanvar_b", [P, H, 2])
        rstd_b = sb("rstd_b", [P, H])
        minus_half = sb("minus_half2", [P, H])
        eps = sb("eps2", [P, H])
        wait_taker = sb("wait_taker2", [P, 3])
        left = sb("left", [P, N])
        right = sb("right", [P, N])
        msg_sum = sb("msg_sum", [P, H, D])
        msg = sb("msg", [P, 2, H, D], F32R)
        expd = sb("expd", [P, H, N])
        att = sb("att", [P, H, N])
        att_s = sb("att_s", [P, 2, H, N], F32R)
        nmp = sb("nmp", [P, 2, H, N], F32R)
        sum_rz = sb("sum_rz", [P, H, 2 * D])
        tanh_rz = sb("tanh_rz", [P, H, 2 * D])
        sum_n = sb("sum_n", [P, H, 2 * D])
        reset = sb("reset", [P, H, D])
        pre_n = sb("pre_n", [P, H, D])
        new = sb("new", [P, H, D])
        x_new = sb("x_new", [P, H, D])
        diff = sb("diff", [P, H, D])
        update = sb("update", [P, H, D])
        h2hat = sb("h2hat", [P, H, D])
        h2t = sb("h2t", [P, 2, H, N], F32R)
        u_s = sb("u_s", [P, 2, H, D], F32R)
        out_sum = sb("out_sum", [P, H, D])
        out_sb = sb("out_sb", [P, 2, H, D])

        ps_s = ps("ps_s")
        ps_b = ps("ps_b")
        ps_adj = ps("ps_adj")
        ps_d = ps("ps_d")
        ps_rz = ps("ps_rz")
        ps_n = ps("ps_n")
        ps_l = [ps(f"ps_l{t}") for t in range(H)]

        x_loaded = [sem(f"x2_loaded{i}") for i in range(2)]
        adj_loaded = [sem(f"adj_loaded{i}") for i in range(2)]
        conv_loaded = [sem(f"conv_loaded{i}") for i in range(2)]
        stored = [sem(f"stored{i}") for i in range(2)]
        names = ("stats1 rstd1_sum rstd1 xhat1 turned1 h_high h_low s_done parts_done msg_done msg_added "
                 "msg_high msg_low adj_turned adj_high adj_low dist_done exp_done att_done att_high att_low "
                 "nmp_done nmp_high nmp_low conv_high conv_low rz_done n_done rz_added n_added rz_tanh "
                 "reset_done pre_done n_tanh x_new_done diff_done update_done x1_done stats2 aggr2 rstd2_sum "
                 "rstd2 h2hat_done turned2 h2_high h2_low l_done u_high u_low out_done out_added out_ready "
                 "bn1 cleared pre_started")
        S = {n: sem("g_" + n) for n in names.split()}

        def ready(e, name, t, n=1, per=1):
            e.wait_ge(S[name], at(t, per, n))

        def before(e, name, t, per=1, back=1):
            if not (isinstance(t, int) and t < back):
                e.wait_ge(S[name], at(t - (back - 1), per, 0))

        def arrived(e, sems, t, p):
            e.wait_ge(sems[p], (t - p) * 8 + 16)

        def load(sp, t, p):
            before(sp, "x1_done", t, H, 2)
            sp.dma_start(xin[:, p, :, :], x_d[t]).then_inc(x_loaded[p], 16)

        def load_rest(sp, t, p):
            before(sp, "adj_turned", t, 1, 2)
            sp.dma_start(adj_in[:, p, :, :], adj_d[t]).then_inc(adj_loaded[p], 16)
            before(sp, "conv_high", t, 1, 2)
            before(sp, "conv_low", t, 1, 2)
            sp.dma_start(conv_in[:, p, :, :], conv_d[t].rearrange("h p n -> p h n")).then_inc(conv_loaded[p], 16)

        def store(sp, t, p):
            ready(sp, "out_ready", t, H, H)
            sp.dma_start(out_d[t], out_sb[:, p, :, :]).then_inc(stored[p], 16)

        def norm1_stats(dve, t, p):
            arrived(dve, x_loaded, t, p)
            for i in range(H):
                dve.bn_stats(stats[:, p, i, :], xin[:, p, i, :]).then_inc(S["bn1"], 1)
            ready(dve, "bn1", t, H, H)
            dve.memset(wait_taker[:, 0:1], 0.0)
            for i in range(H):
                last = dve.bn_aggr(meanvar[:, p, i, :], stats[:, p, i, :])
            last.then_inc(S["stats1"], 1)

        def norm1_rstd(pool, t, p):
            ready(pool, "stats1", t)
            pool.tensor_tensor(rstd[:, p, :], meanvar[:, p, :, 1], eps[:, :], ALU.add).then_inc(S["rstd1_sum"], 1)
            ready(pool, "rstd1_sum", t)
            pool.tensor_tensor(rstd[:, p, :], rstd[:, p, :], minus_half[:, :], ALU.pow).then_inc(S["rstd1"], 1)

        def norm1(dve, t, p):
            ready(dve, "rstd1", t)
            for i in range(H):
                last = dve.tensor_scalar(xhat[:, p, i, :], xin[:, p, i, :], meanvar[:, p, i, 0:1],
                                         rstd[:, p, i:i + 1], ALU.subtract, ALU.mult)
            last.then_inc(S["xhat1"], 1)

        def turn1(pe, t, p):
            ready(pe, "xhat1", t)
            before(pe, "parts_done", t)
            for kh in range(H):
                for i in range(H):
                    last = pe.transpose(ps_s[:, kh * N + i * P:kh * N + i * P + P],
                                        xhat[:, p, i, kh * P:kh * P + P], ident[:, :])
            last.then_inc(S["turned1"], 1)

        def h_split_high(act, t, p):
            ready(act, "turned1", t)
            act.activation(ht[:, p, 0, :, :].rearrange("p h n -> p (h n)"), ps_s[:, :],
                           ACT.Relu).then_inc(S["h_high"], 1)

        def h_split_low(dve, t, p):
            ready(dve, "h_high", t)
            dve.scalar_tensor_tensor(out=ht[:, p, 1, :, :].rearrange("p h n -> p (h n)"), in0=ps_s[:, :], scalar=0.0,
                                     in1=ht[:, p, 0, :, :].rearrange("p h n -> p (h n)").bitcast(F32),
                                     op0=ALU.max, op1=ALU.subtract).then_inc(S["h_low"], 1)

        def conv_split_high(act, t, p):
            arrived(act, conv_loaded, t, p)
            before(act, "n_done", t, H, 2)
            act.activation(conv_t[:, p, 0, :, :], conv_in[:, p, :, :], ACT.Copy).then_inc(S["conv_high"], 1)

        def conv_split_low(pool, t, p):
            ready(pool, "conv_high", t)
            pool.tensor_tensor(conv_t[:, p, 1, :, :], conv_in[:, p, :, :], conv_t[:, p, 0, :, :].bitcast(F32),
                               ALU.subtract).then_inc(S["conv_low"], 1)

        def three(pe, dest, stationary, moving, start, stop, **kw):
            for n, (wl, dl) in enumerate(PASSES):
                last = pe.matmul(dest, stationary(dl), moving(wl), start=start and n == 0, stop=stop and n == 2, **kw)
            return last

        def small(pe, t, p):
            ready(pe, "h_low", t)
            for kh in range(H):
                last = three(pe, ps_s[:, 0:N], lambda s: w["se"][:, s, kh, :], lambda s: ht[:, p, s, kh, :],
                             kh == 0, kh == H - 1)
            last.then_inc(S["s_done"], 1)

        def parts(act, t, p):
            ready(act, "s_done", t)
            before(act, "dist_done", t)
            b = w["bias_se"]
            act.activation(left[0:32, :], ps_s[0:32, 0:N], ACT.Identity, bias=b[0:32, :])
            act.activation(right[0:32, :], ps_s[0:32, 0:N], ACT.Identity, bias=b[0:32, :])
            act.activation(left[64:96, :], ps_s[64:96, 0:N], ACT.Square, bias=b[64:96, :])
            act.activation(right[32:64, :], ps_s[32:64, 0:N], ACT.Square,
                           bias=b[32:64, :]).then_inc(S["parts_done"], 1)

        def distances(pe, t, p):
            ready(pe, "parts_done", t)
            if not (isinstance(t, int) and t < 2):
                ready(pe, "h2_low", t - 2)
            for i in range(H):
                last = pe.matmul(ps_d[:, i * N:i * N + N], left[:, i * P:i * P + P], right[:, :], start=True, stop=True)
            last.then_inc(S["dist_done"], 1)

        def exponential(act, t, p):
            ready(act, "dist_done", t)
            before(act, "att_done", t)
            act.activation(expd[:, :, :].rearrange("p h n -> p (h n)"), ps_d[:, :], ACT.Exp,
                           scale=2.0).then_inc(S["exp_done"], 1)

        def turn_adj(pe, t, p):
            arrived(pe, adj_loaded, t, p)
            before(pe, "att_done", t)
            before(pe, "adj_low", t)
            for m in range(H):
                for i in range(H):
                    last = pe.transpose(ps_adj[:, m * N + i * P:m * N + i * P + P],
                                        adj_in[:, p, i, m * P:m * P + P], ident[:, :])
            last.then_inc(S["adj_turned"], 1)

        def adj_split_high(act, t, p):
            ready(act, "adj_turned", t)
            before(act, "out_done", t, H, 2)
            act.activation(adj_t[:, p, 0, :, :].rearrange("p h n -> p (h n)"), ps_adj[:, :],
                           ACT.Copy).then_inc(S["adj_high"], 1)

        def adj_split_low(dve, t, p):
            ready(dve, "adj_high", t)
            dve.tensor_tensor(adj_t[:, p, 1, :, :].rearrange("p h n -> p (h n)"), ps_adj[:, :],
                              adj_t[:, p, 0, :, :].rearrange("p h n -> p (h n)").bitcast(F32),
                              ALU.subtract).then_inc(S["adj_low"], 1)

        def attention(dve, t, p):
            ready(dve, "exp_done", t)
            before(dve, "att_high", t)
            before(dve, "att_low", t)
            dve.tensor_tensor(att[:, :, :].rearrange("p h n -> p (h n)"),
                              ps_adj[:, :], expd[:, :, :].rearrange("p h n -> p (h n)"),
                              ALU.mult).then_inc(S["att_done"], 1)

        def att_split_high(act, t, p):
            ready(act, "att_done", t)
            before(act, "nmp_done", t)
            act.activation(att_s[:, 0, :, :], att[:, :, :], ACT.Copy).then_inc(S["att_high"], 1)

        def att_split_low(pool, t, p):
            ready(pool, "att_high", t)
            pool.tensor_tensor(att_s[:, 1, :, :], att[:, :, :], att_s[:, 0, :, :].bitcast(F32),
                               ALU.subtract).then_inc(S["att_low"], 1)

        def messages(pe, t, p):
            before(pe, "nmp_low", t)
            for i in range(H):
                for kh in range(H):
                    last = three(pe, ps_b[:, i * D:i * D + D], lambda s: ht[:, p, s, kh, i * P:i * P + P],
                                 lambda s: w["msg"][:, s, kh, :], kh == 0, kh == H - 1)
            last.then_inc(S["msg_done"], 1)

        def messages_add(dve, t, p):
            ready(dve, "msg_done", t)
            before(dve, "msg_high", t)
            dve.tensor_tensor(msg_sum[:, :, :].rearrange("p h d -> p (h d)"), ps_b[:, :],
                              w["bias_msg"][:, :, :].rearrange("p h d -> p (h d)"),
                              ALU.add).then_inc(S["msg_added"], 1)

        def messages_high(act, t, p):
            ready(act, "msg_added", t)
            before(act, "nmp_done", t)
            act.activation(msg[:, 0, :, :], msg_sum[:, :, :], ACT.Relu).then_inc(S["msg_high"], 1)

        def messages_low(dve, t, p):
            ready(dve, "msg_high", t)
            dve.scalar_tensor_tensor(out=msg[:, 1, :, :], in0=msg_sum[:, :, :], scalar=0.0,
                                     in1=msg[:, 0, :, :].bitcast(F32), op0=ALU.max,
                                     op1=ALU.subtract).then_inc(S["msg_low"], 1)

        def weighted(pe, t, p):
            ready(pe, "msg_low", t)
            ready(pe, "att_low", t)
            for dh in range(H):
                for m in range(H):
                    last = three(pe, ps_b[:, dh * N:dh * N + N], lambda s: msg[:, s, m, dh * P:dh * P + P],
                                 lambda s: att_s[:, s, m, :], m == 0, m == H - 1)
            last.then_inc(S["nmp_done"], 1)

        def weighted_high(act, t, p):
            ready(act, "nmp_done", t)
            before(act, "n_done", t, H)
            act.activation(nmp[:, 0, :, :].rearrange("p h n -> p (h n)"), ps_b[:, :],
                           ACT.Copy).then_inc(S["nmp_high"], 1)

        def weighted_low(dve, t, p):
            ready(dve, "nmp_high", t)
            dve.tensor_tensor(nmp[:, 1, :, :].rearrange("p h n -> p (h n)"), ps_b[:, :],
                              nmp[:, 0, :, :].rearrange("p h n -> p (h n)").bitcast(F32),
                              ALU.subtract).then_inc(S["nmp_low"], 1)

        def gates_first(pe, t, p, i):
            if i == 0:
                ready(pe, "conv_low", t)
            ready(pe, "rz_added", t, i, H)
            ready(pe, "n_added", t, i, H)
            for kh in range(H):
                three(pe, ps_rz[:, :], lambda s: ht[:, p, s, kh, i * P:i * P + P],
                      lambda s: w["hh"][:, s, kh, 0:2 * D], kh == 0, False)
            for kh in range(H):
                three(pe, ps_n[:, D:2 * D], lambda s: ht[:, p, s, kh, i * P:i * P + P],
                      lambda s: w["hh"][:, s, kh, 2 * D:3 * D], kh == 0, False, skip_group_check=True)
            for kh in range(H):
                three(pe, ps_rz[:, :], lambda s: conv_t[:, p, s, kh, i * P:i * P + P],
                      lambda s: w["ih"][:, s, kh, 0:2 * D], False, False)
            for kh in range(H):
                three(pe, ps_n[:, 0:D], lambda s: conv_t[:, p, s, kh, i * P:i * P + P],
                      lambda s: w["ih"][:, s, kh, 2 * D:3 * D], False, False, skip_group_check=True)

        def gates_second(pe, t, p, i):
            if i == 0:
                ready(pe, "nmp_low", t)
            for kh in range(H):
                last = three(pe, ps_rz[:, :], lambda s: nmp[:, s, kh, i * P:i * P + P],
                             lambda s: w["ih"][:, s, 2 + kh, 0:2 * D], False, kh == H - 1)
            last.then_inc(S["rz_done"], 1)
            for kh in range(H):
                last = three(pe, ps_n[:, 0:D], lambda s: nmp[:, s, kh, i * P:i * P + P],
                             lambda s: w["ih"][:, s, 2 + kh, 2 * D:3 * D], False, kh == H - 1, skip_group_check=True)
            last.then_inc(S["n_done"], 1)

        def gate_sums(dve, t, p, i):
            ready(dve, "rz_done", t, i + 1, H)
            before(dve, "rz_tanh", t, H)
            dve.tensor_tensor(sum_rz[:, i, :], ps_rz[:, :], w["bias_rz"][:, :], ALU.add).then_inc(S["rz_added"], 1)
            ready(dve, "n_done", t, i + 1, H)
            before(dve, "pre_done", t, H)
            dve.tensor_tensor(sum_n[:, i, :], ps_n[:, :], w["bias_n"][:, :], ALU.add).then_inc(S["n_added"], 1)

        def gate_tanh(act, t, p, i):
            ready(act, "rz_added", t, i + 1, H)
            before(act, "update_done", t, H)
            act.activation(tanh_rz[:, i, :], sum_rz[:, i, :], ACT.Tanh, scale=0.5).then_inc(S["rz_tanh"], 1)

        def gate_new(dve, t, p, i):
            ready(dve, "rz_tanh", t, i + 1, H)
            ready(dve, "n_added", t, i + 1, H)
            before(dve, "n_tanh", t, H)
            dve.scalar_tensor_tensor(out=reset[:, i, :], in0=tanh_rz[:, i, 0:D], scalar=1.0, in1=sum_n[:, i, D:2 * D],
                                     op0=ALU.add, op1=ALU.mult).then_inc(S["reset_done"], 1)
            ready(dve, "reset_done", t, i + 1, H)
            dve.scalar_tensor_tensor(out=pre_n[:, i, :], in0=reset[:, i, :], scalar=0.5, in1=sum_n[:, i, 0:D],
                                     op0=ALU.mult, op1=ALU.add).then_inc(S["pre_done"], 1)

        def new_tanh(act, t, p, i):
            ready(act, "pre_done", t, i + 1, H)
            before(act, "x_new_done", t, H)
            before(act, "diff_done", t, H)
            act.activation(new[:, i, :], pre_n[:, i, :], ACT.Tanh).then_inc(S["n_tanh"], 1)

        def add_new(pool, t, p, i):
            ready(pool, "n_tanh", t, i + 1, H)
            before(pool, "x1_done", t, H)
            pool.tensor_tensor(x_new[:, i, :], xin[:, p, i, :], new[:, i, :], ALU.add).then_inc(S["x_new_done"], 1)

        def new_rows(dve, t, p, i):
            ready(dve, "n_tanh", t, i + 1, H)
            dve.scalar_tensor_tensor(out=diff[:, i, :], in0=xhat[:, p, i, :], scalar=0.0, in1=new[:, i, :],
                                     op0=ALU.max, op1=ALU.subtract).then_inc(S["diff_done"], 1)
            ready(dve, "diff_done", t, i + 1, H)
            dve.scalar_tensor_tensor(out=update[:, i, :], in0=tanh_rz[:, i, D:2 * D], scalar=1.0, in1=diff[:, i, :],
                                     op0=ALU.add, op1=ALU.mult).then_inc(S["update_done"], 1)
            ready(dve, "update_done", t, i + 1, H)
            ready(dve, "x_new_done", t, i + 1, H)
            dve.scalar_tensor_tensor(out=x1[:, p, i, :], in0=update[:, i, :], scalar=0.5, in1=x_new[:, i, :],
                                     op0=ALU.mult, op1=ALU.add).then_inc(S["x1_done"], 1)
            ready(dve, "x1_done", t, i + 1, H)
            dve.bn_stats(stats_b[:, i, :], x1[:, p, i, :]).then_inc(S["stats2"], 1)
            ready(dve, "stats2", t, i + 1, H)
            dve.memset(wait_taker[:, 1 + i:2 + i], 0.0)
            dve.bn_aggr(meanvar_b[:, i, :], stats_b[:, i, :]).then_inc(S["aggr2"], 1)

        def norm2_rstd(pool, t, p):
            ready(pool, "aggr2", t, H, H)
            pool.tensor_tensor(rstd_b[:, :], meanvar_b[:, :, 1], eps[:, :], ALU.add).then_inc(S["rstd2_sum"], 1)
            ready(pool, "rstd2_sum", t)
            pool.tensor_tensor(rstd_b[:, :], rstd_b[:, :], minus_half[:, :], ALU.pow).then_inc(S["rstd2"], 1)

        def norm2(dve, t, p):
            ready(dve, "rstd2", t)
            before(dve, "turned2", t)
            for i in range(H):
                last = dve.tensor_scalar(h2hat[:, i, :], x1[:, p, i, :], meanvar_b[:, i, 0:1], rstd_b[:, i:i + 1],
                                         ALU.subtract, ALU.mult)
            last.then_inc(S["h2hat_done"], 1)

        def turn2(pe, t, p, more):
            ready(pe, "h2hat_done", t)
            if more:
                ready(pe, "exp_done", t + 1)
            for kh in range(H):
                for i in range(H):
                    last = pe.transpose(ps_d[:, kh * N + i * P:kh * N + i * P + P],
                                        h2hat[:, i, kh * P:kh * P + P], ident[:, :])
            last.then_inc(S["turned2"], 1)

        def h2_split_high(act, t, p):
            ready(act, "turned2", t)
            before(act, "l_done", t)
            act.activation(h2t[:, 0, :, :].rearrange("p h n -> p (h n)"), ps_d[:, :],
                           ACT.Relu).then_inc(S["h2_high"], 1)

        def h2_split_low(dve, t, p):
            ready(dve, "h2_high", t)
            dve.scalar_tensor_tensor(out=h2t[:, 1, :, :].rearrange("p h n -> p (h n)"), in0=ps_d[:, :], scalar=0.0,
                                     in1=h2t[:, 0, :, :].rearrange("p h n -> p (h n)").bitcast(F32),
                                     op0=ALU.max, op1=ALU.subtract).then_inc(S["h2_low"], 1)

        def layer1(pe, t, p):
            ready(pe, "h2_low", t)
            before(pe, "out_added", t, H)
            for i in range(H):
                for kh in range(H):
                    last = three(pe, ps_l[i][:, :], lambda s: h2t[:, s, kh, i * P:i * P + P],
                                 lambda s: w["l1"][:, s, kh, :], kh == 0, kh == H - 1)
            last.then_inc(S["l_done"], 1)

        def passed_high(act, t, p):
            ready(act, "l_done", t)
            before(act, "out_done", t, H)
            for i in range(H):
                act.activation(u_s[:, 0, i, :], ps_l[i][:, D:2 * D], ACT.Copy).then_inc(S["u_high"], 1)

        def passed_low(dve, t, p):
            for i in range(H):
                ready(dve, "u_high", t, i + 1, H)
                dve.tensor_tensor(u_s[:, 1, i, :], ps_l[i][:, D:2 * D], u_s[:, 0, i, :].bitcast(F32),
                                  ALU.subtract).then_inc(S["u_low"], 1)

        def neighbours(pe, t, p):
            ready(pe, "u_low", t, H, H)
            for i in range(H):
                for m in range(H):
                    last = three(pe, ps_l[i][:, 0:D], lambda s: adj_t[:, p, s, m, i * P:i * P + P],
                                 lambda s: u_s[:, s, m, :], False, m == H - 1, skip_group_check=True)
                last.then_inc(S["out_done"], 1)

        def finish(dve, t, p):
            if not (isinstance(t, int) and t < 2):
                dve.wait_ge(stored[p], (t - p) * 8)
            for i in range(H):
                ready(dve, "out_done", t, i + 1, H)
                dve.tensor_tensor(out_sum[:, i, :], ps_l[i][:, 0:D], w["bias_out"][:, :],
                                  ALU.add).then_inc(S["out_added"], 1)
                ready(dve, "out_added", t, i + 1, H)
                dve.scalar_tensor_tensor(out=out_sb[:, p, i, :], in0=out_sum[:, i, :], scalar=0.0, in1=x1[:, p, i, :],
                                         op0=ALU.max, op1=ALU.add).then_inc(S["out_ready"], 1)

        def slots(engine, slot):
            slot(0, 0, False, True, True)
            slot(1, 1, True, True, True)
            with engine.Fori(1, (graphs - 2) // 2) as j:
                for p in range(2):
                    slot(j * 2 + p, p, True, True, True)
            slot(graphs - 2, 0, True, True, True)
            slot(graphs - 1, 1, True, True, False)
            slot(graphs, 0, True, False, False)

        with nc.Block() as block:
            @block.sync
            def _(sp):
                load(sp, 0, 0)
                load_rest(sp, 0, 0)
                load(sp, 1, 1)

                def slot(t, p, prev, cur, nxt):
                    if nxt:
                        load_rest(sp, t + 1, 1 - p)
                    if prev and nxt:
                        load(sp, t + 1, 1 - p)
                    if prev:
                        store(sp, t - 1, 1 - p)

                slots(sp, slot)
                for i in range(2):
                    sp.wait_ge(stored[i], graphs * 8)

            @block.gpsimd
            def _(pool):
                pool.memset(minus_half[:, :], -0.5).then_inc(S["cleared"], 1)
                pool.memset(eps[:, :], EPS).then_inc(S["cleared"], 1)
                pool.wait_ge(S["cleared"], 8)
                norm1_rstd(pool, 0, 0)
                conv_split_low(pool, 0, 0)

                def slot(t, p, prev, cur, nxt):
                    if prev:
                        add_new(pool, t - 1, 1 - p, 1)
                        norm2_rstd(pool, t - 1, 1 - p)
                    if cur:
                        att_split_low(pool, t, p)
                    if nxt:
                        norm1_rstd(pool, t + 1, 1 - p)
                        conv_split_low(pool, t + 1, 1 - p)
                    if cur:
                        add_new(pool, t, p, 0)

                slots(pool, slot)

            @block.scalar
            def _(act):
                act.wait_ge(S["cleared"], 8)
                h_split_high(act, 0, 0)
                conv_split_high(act, 0, 0)

                def slot(t, p, prev, cur, nxt):
                    if prev:
                        gate_tanh(act, t - 1, 1 - p, 1)
                    if cur:
                        parts(act, t, p)
                    if prev:
                        new_tanh(act, t - 1, 1 - p, 1)
                    if cur:
                        adj_split_high(act, t, p)
                        messages_high(act, t, p)
                        exponential(act, t, p)
                        att_split_high(act, t, p)
                    if prev:
                        h2_split_high(act, t - 1, 1 - p)
                    if cur:
                        weighted_high(act, t, p)
                    if prev:
                        passed_high(act, t - 1, 1 - p)
                    if nxt:
                        conv_split_high(act, t + 1, 1 - p)
                    if cur:
                        gate_tanh(act, t, p, 0)
                        new_tanh(act, t, p, 0)
                    if nxt:
                        h_split_high(act, t + 1, 1 - p)

                slots(act, slot)

            @block.vector
            def _(dve):
                for side, row in ((left, 32), (right, 64)):
                    dve.memset(side[row:row + 32, :], -0.5).then_inc(S["cleared"], 1)
                    dve.memset(side[96:128, :], 0.0).then_inc(S["cleared"], 1)
                dve.memset(left[0:32, :], 0.0).then_inc(S["cleared"], 1)
                dve.memset(right[0:32, :], 0.0).then_inc(S["cleared"], 1)
                dve.wait_ge(S["cleared"], 8)
                norm1_stats(dve, 0, 0)
                norm1(dve, 0, 0)
                h_split_low(dve, 0, 0)

                def slot(t, p, prev, cur, nxt):
                    if prev:
                        gate_sums(dve, t - 1, 1 - p, 1)
                        gate_new(dve, t - 1, 1 - p, 1)
                    if cur:
                        messages_add(dve, t, p)
                        adj_split_low(dve, t, p)
                    if prev:
                        new_rows(dve, t - 1, 1 - p, 1)
                    if cur:
                        messages_low(dve, t, p)
                        attention(dve, t, p)
                    if prev:
                        norm2(dve, t - 1, 1 - p)
                    if nxt:
                        norm1_stats(dve, t + 1, 1 - p)
                    if prev:
                        h2_split_low(dve, t - 1, 1 - p)
                    if cur:
                        weighted_low(dve, t, p)
                    if nxt:
                        norm1(dve, t + 1, 1 - p)
                    if prev:
                        passed_low(dve, t - 1, 1 - p)
                    if cur:
                        gate_sums(dve, t, p, 0)
                        gate_new(dve, t, p, 0)
                        new_rows(dve, t, p, 0)
                    if prev:
                        finish(dve, t - 1, 1 - p)
                    if nxt:
                        h_split_low(dve, t + 1, 1 - p)

                slots(dve, slot)

            @block.tensor
            def _(pe):
                turn1(pe, 0, 0)

                def slot(t, p, prev, cur, nxt):
                    if cur:
                        small(pe, t, p)
                        messages(pe, t, p)
                        turn_adj(pe, t, p)
                        distances(pe, t, p)
                        gates_first(pe, t, p, 0)
                    if prev:
                        turn2(pe, t - 1, 1 - p, cur)
                    if cur:
                        weighted(pe, t, p)
                    if prev:
                        layer1(pe, t - 1, 1 - p)
                    if cur:
                        gates_second(pe, t, p, 0)
                    if prev:
                        neighbours(pe, t - 1, 1 - p)
                    if cur:
                        gates_first(pe, t, p, 1)
                    if nxt:
                        turn1(pe, t + 1, 1 - p)
                    if cur:
                        gates_second(pe, t, p, 1)

                slots(pe, slot)


GATE_TILES = {
    "ih": ([P, 2, 4, 3 * D], F32R),
    "hh": ([P, 2, H, 3 * D], F32R),
    "msg": ([P, 2, H, D], F32R),
    "l1": ([P, 2, H, 2 * D], F32R),
    "se": ([P, 2, H, P], F32R),
    "bias_se": ([P, 1], F32),
    "bias_rz": ([P, 2 * D], F32),
    "bias_n": ([P, 2 * D], F32),
    "bias_out": ([P, D], F32),
    "bias_msg": ([P, H, D], F32),
}


def build(nc, a, out):
    graphs = a["x"].shape[0]
    conv_out = nc.dram_tensor("conv_out", (graphs // G, G, H, P, N), F32).ap()
    with nc.sbuf_tensor("ident", [P, P], F32) as ident:
        with (
            nc.sbuf_tensor("w2", [P, 2, 37, H, D], F16) as w2,
            nc.sbuf_tensor("w1t", [P, 2, H, D], F32R) as w1t,
            nc.sbuf_tensor("cvec", [P, 8], F32) as cvec,
        ):
            convolution_weights(nc, ident, w2, w1t, cvec, a["conv1_w"], a["conv2_w"],
                                [a[f"bn1_{s}"] for s in "gbmv"], [a[f"bn2_{s}"] for s in "gbmv"])
            convolution(nc, ident, w2, w1t, cvec, a["x"], conv_out)
        with ExitStack() as ctx:
            w = {n: ctx.enter_context(nc.sbuf_tensor("w_" + n, s, dt)) for n, (s, dt) in GATE_TILES.items()}
            gate_weights(nc, ident, w, a)
            gates(nc, ident, w, a["x"], a["adj"], conv_out, out)


def kernel(**inputs):
    import numpy as np
    from concourse import bacc
    from concourse.bass_utils import run_bass_kernel_spmd

    nc = bacc.Bacc("TRN2", target_bir_lowering=False, num_devices=1)
    arrays, args = {}, {}
    for name, value in inputs.items():
        value = np.ascontiguousarray(value)
        short = name.replace("L0_gnn_", "").replace("L1_gnn_weight", "l1_w").replace("L1_gnn_bias", "l1_b")
        arrays[f"in_{short}"] = value
        args[short] = nc.dram_tensor(f"in_{short}", value.shape, mybir.dt.from_np(value.dtype),
                                     kind="ExternalInput").ap()
    x = args["x"]
    out = nc.dram_tensor("out", x.shape, F32, kind="ExternalOutput").ap()
    build(nc, args, out)
    result = run_bass_kernel_spmd(nc, [arrays], core_ids=[0])
    return result.results[0]["out"]
```
